# Optimizing a Trainium2 kernel written in Bass

```python
import numpy as np
import jax
import jax.numpy as jnp

def _softmax(x, axis=-1):
    return jax.nn.softmax(x, axis=axis)

def _gelu(x):
    return jax.nn.gelu(x, approximate=True)

def _silu(x):
    return jax.nn.silu(x)

def _sigmoid(x):
    return jax.nn.sigmoid(x)

def _layernorm(x, axis=-1, eps=1e-05):
    m = jnp.mean(x, axis=axis, keepdims=True)
    v = jnp.var(x, axis=axis, keepdims=True)
    return (x - m) / jnp.sqrt(v + eps)

def _scatter_add(tgt, idx, src, axis=0):
    return tgt.at[idx].add(src)

def _segment_sum(src, seg, n):
    return jax.ops.segment_sum(src, seg, n)
kernel_name = 'mk_cond_resid_d1_seqx_r4_d18104'

def setup_inputs(seed: int=0):
    np.random.seed(seed)
    _w = jnp.asarray

    def _rec_inputs():
        import jax
        import jax.numpy as jnp
        _rk = jax.random.key(seed)
        x = -0.0005207 + 1.001 * jax.random.normal(jax.random.fold_in(_rk, 1), (64, 64, 256), jnp.float32)
        _lenS = 64 - jax.random.randint(jax.random.fold_in(_rk, 7), (64,), 0, max(1, 64 // 4) + 1, jnp.int32)
        _lenS2 = 64 - jax.random.randint(jax.random.fold_in(_rk, 8), (64,), 0, max(1, 64 // 4) + 1, jnp.int32)
        fside_Bx8_0 = jax.random.uniform(jax.random.fold_in(_rk, 11), (64, 8), jnp.float32, 0.0, 0.556406)
        condB_sharedgateprob = jax.random.uniform(jax.random.fold_in(_rk, 12), (64,), jnp.float32, 0.0, 0.794948)
        return (x, fside_Bx8_0, condB_sharedgateprob)
    x, fside_Bx8_0, condB_sharedgateprob = _rec_inputs()

    def _L0_cond_setup():
        import jax, jax.numpy as jnp
        import numpy as np
        E, B, S, D, F = (8, 2, 256, 256, 1024)
        key = jax.random.key(seed)
        ks = jax.random.split(key, 9)
        sc_d = 1.0 / np.sqrt(D)
        sc_f = 1.0 / np.sqrt(F)
        hidden_states = jax.random.normal(ks[0], (B, S, D), dtype=jnp.float32)
        gating_probs = jax.nn.softmax(jax.random.normal(ks[1], (B, E), dtype=jnp.float32), axis=-1)
        shared_gate_prob = jax.nn.sigmoid(jax.random.normal(ks[2], (B, 1), dtype=jnp.float32))
        Wg = jax.random.normal(ks[3], (E, D, F), dtype=jnp.float32) * sc_d
        Wu = jax.random.normal(ks[4], (E, D, F), dtype=jnp.float32) * sc_d
        Wd = jax.random.normal(ks[5], (E, F, D), dtype=jnp.float32) * sc_f
        Sg = jax.random.normal(ks[6], (D, F), dtype=jnp.float32) * sc_d
        Su = jax.random.normal(ks[7], (D, F), dtype=jnp.float32) * sc_d
        Sd = jax.random.normal(ks[8], (F, D), dtype=jnp.float32) * sc_f
        return {'hidden_states': hidden_states, 'gating_probs': gating_probs, 'shared_gate_prob': shared_gate_prob, 'Wg': Wg, 'Wu': Wu, 'Wd': Wd, 'Sg': Sg, 'Su': Su, 'Sd': Sd}
    _L0_cond_all = _L0_cond_setup()
    _L0_cond_in = {k: v for k, v in _L0_cond_all.items() if k in ('Wg', 'Wu', 'Wd', 'Sg', 'Su', 'Sd')}
    del _L0_cond_all
    return {'x': x, 'fside_Bx8_0': fside_Bx8_0, 'condB_sharedgateprob': condB_sharedgateprob, 'L0_cond_Wg': _L0_cond_in['Wg'], 'L0_cond_Wu': _L0_cond_in['Wu'], 'L0_cond_Wd': _L0_cond_in['Wd'], 'L0_cond_Sg': _L0_cond_in['Sg'], 'L0_cond_Su': _L0_cond_in['Su'], 'L0_cond_Sd': _L0_cond_in['Sd']}

def reference(x, fside_Bx8_0, condB_sharedgateprob, L0_cond_Wg, L0_cond_Wu, L0_cond_Wd, L0_cond_Sg, L0_cond_Su, L0_cond_Sd):
    import jax
    import jax.numpy as jnp

    def _L0_cond_ref(hidden_states, gating_probs, shared_gate_prob, Wg, Wu, Wd, Sg, Su, Sd):
        import jax, jax.numpy as jnp
        import numpy as np
        E, B, S, D, F = (8, 2, 256, 256, 1024)
        h = hidden_states
        g = jnp.einsum('bsd,edf->ebsf', h, Wg)
        u = jnp.einsum('bsd,edf->ebsf', h, Wu)
        expert_outs = jnp.einsum('ebsf,efd->ebsd', jax.nn.silu(g) * u, Wd)
        expert_output = jnp.einsum('be,ebsd->bsd', gating_probs, expert_outs)
        shared = jnp.einsum('bsf,fd->bsd', jax.nn.silu(h @ Sg) * (h @ Su), Sd)
        sg = shared_gate_prob[:, :, None]
        return (1.0 - sg) * expert_output + sg * shared
    x = x + _L0_cond_ref(x, fside_Bx8_0, condB_sharedgateprob[:, None], L0_cond_Wg, L0_cond_Wu, L0_cond_Wd, L0_cond_Sg, L0_cond_Su, L0_cond_Sd)
    return x

_drawn_inputs = setup_inputs


def setup_inputs(seed=0):
    import zlib

    import numpy as np

    out = dict(_drawn_inputs(seed))
    spreads = {}
    factors = {}
    for name, (base, spread) in spreads.items():
        noise = np.random.default_rng([zlib.crc32(name.encode()), seed]).standard_normal(out[name].shape)
        drawn = base * np.exp(spread * noise) if base else spread * noise
        out[name] = jnp.asarray(drawn.astype(out[name].dtype))
    for name, factor in factors.items():
        out[name] = (out[name] * factor).astype(out[name].dtype)
    return out
```

```python
from contextlib import ExitStack

import concourse.bass as bass
from concourse import mybir

F32 = mybir.dt.float32
F32R = mybir.dt.float32r
ALU = mybir.AluOpType
ACT = mybir.ActivationFunctionType

P = 128
TB = 512


def not_first(b):
    return not (isinstance(b, int) and b == 0)


def moe_program(nc, x_dram, gating_dram, shared_dram, w_dram, out_dram):
    NT, _, K, _ = x_dram.shape
    NE, NF, _, SLICE = w_dram.shape
    BATCH = shared_dram.shape[0]
    SEQ = NT * TB // BATCH
    BPB = TB // SEQ
    NB = NE * NT
    D = K * P

    with ExitStack() as ctx:
        def sb(name, shape, dt=F32):
            return ctx.enter_context(nc.sbuf_tensor(name, shape, dt))

        def sem(name):
            return ctx.enter_context(nc.semaphore(name))

        out_acc = sb("out_acc", [P, NT * K * TB])
        x_hi = sb("x_hi", [P, NT * K * TB], F32R)
        x_lo = sb("x_lo", [P, NT * K * TB], F32R)
        w_stage = sb("w_stage", [P, NF, SLICE])
        w_hi = sb("w_hi", [P, NF, SLICE], F32R)
        w_lo = sb("w_lo", [P, NF, SLICE], F32R)
        h = sb("h", [P, 2, TB])
        h_hi = sb("h_hi", [P, 2, TB], F32R)
        h_lo = sb("h_lo", [P, 2, TB], F32R)
        scaled = sb("scaled", [P, K * TB])
        zero = sb("zero", [P, 1])
        gates = sb("gates", [P, BATCH, NE - 1])
        coef = sb("coef", [P, NE * BATCH])
        one_minus = sb("one_minus", [P, BATCH])

        g_ps = ctx.enter_context(nc.psum_tensor("g_ps", [P, 2, TB], F32))
        u_ps = ctx.enter_context(nc.psum_tensor("u_ps", [P, 2, TB], F32))
        down_ps = ctx.enter_context(nc.psum_tensor("down_ps", [P, K, TB], F32))

        x_landed = [sem(f"x_landed{t}") for t in range(NT)]
        w_landed = [sem(f"w_landed{s}") for s in range(NF)]
        gates_landed = sem("gates_landed")
        gates_step = sem("gates_step")
        coef_ready = sem("coef_ready")
        zero_set = sem("zero_set")
        x_hi_done = sem("x_hi_done")
        x_ready = sem("x_ready")
        w_hi_done = sem("w_hi_done")
        w_ready = sem("w_ready")
        g_done = sem("g_done")
        u_done = sem("u_done")
        silu_done = sem("silu_done")
        h_done = sem("h_done")
        h_hi_done = sem("h_hi_done")
        h_lo_done = sem("h_lo_done")
        down_done = sem("down_done")
        scaled_done = sem("scaled_done")
        acc_done = sem("acc_done")
        stored = sem("stored")

        block = ctx.enter_context(nc.Block())
        XB = K * TB

        @block.sync
        def _(sp):
            def load_slice(e, s):
                sp.dma_start(w_stage[:, s, :], w_dram[e, s]).then_inc(w_landed[s], 16)

            def load_x(t):
                sp.dma_start(out_acc[:, t * XB:(t + 1) * XB],
                             x_dram[t].rearrange("p k n -> p (k n)")).then_inc(x_landed[t], 16)

            load_x(0)
            for s in range(NF):
                load_slice(0, s)
            sp.dma_start(gates[:].rearrange("p b e -> p (b e)"),
                         gating_dram.rearrange("b e -> (b e)").partition_broadcast(P)).then_inc(gates_landed, 16)
            sp.dma_start(coef[:, (NE - 1) * BATCH:], shared_dram.partition_broadcast(P)).then_inc(gates_landed, 16)
            for t in range(1, NT):
                load_x(t)
            with sp.Fori(1, NE) as e:
                for s in range(NF):
                    sp.wait_ge(w_ready, (e - 1) * NF + (s + 1))
                    sp.dma_start(w_stage[:, s, :], w_dram[bass.ds(e, 1), s].rearrange("a p n -> (a p) n")
                                 ).then_inc(w_landed[s], 16)
            for t in range(NT):
                sp.wait_ge(acc_done, NB - NT + t + 1)
                sp.dma_start(out_dram[t].rearrange("p k n -> p (k n)"),
                             out_acc[:, t * XB:(t + 1) * XB]).then_inc(stored, 16)
            sp.wait_ge(stored, 16 * NT)

        @block.gpsimd
        def _(pool):
            def split_x(t):
                c = slice(t * XB, (t + 1) * XB)
                pool.wait_ge(x_landed[t], 16)
                nc.gpsimd.tensor_copy(x_hi[:, c], out_acc[:, c]).then_inc(x_hi_done, 1)
                pool.wait_ge(x_hi_done, t + 1)
                nc.gpsimd.tensor_tensor(x_lo[:, c], out_acc[:, c], x_hi[:, c].bitcast(F32),
                                        ALU.subtract).then_inc(x_ready, 1)

            def split_slice(s, done):
                nc.gpsimd.tensor_tensor(w_hi[:, s, :], w_stage[:, s, :], zero[:, 0:1].to_broadcast([P, SLICE]),
                                        ALU.subtract).then_inc(w_hi_done, 1)
                pool.wait_ge(w_hi_done, done + 1)
                nc.gpsimd.tensor_tensor(w_lo[:, s, :], w_stage[:, s, :], w_hi[:, s, :].bitcast(F32),
                                        ALU.subtract).then_inc(w_ready, 1)

            nc.gpsimd.memset(zero[:], 0.0).then_inc(zero_set, 1)
            pool.wait_ge(zero_set, 1)
            split_x(0)
            for s in range(NF):
                pool.wait_ge(w_landed[s], 16)
                split_slice(s, s)
            for t in range(1, NT):
                split_x(t)
            with pool.Fori(1, NE) as e:
                for s in range(NF):
                    pool.wait_ge(w_landed[s], e * 16 + 16)
                    pool.wait_ge(down_done, e * (NT * NF) + (s + 1 - NF))
                    split_slice(s, e * NF + s)

        @block.tensor
        def _(pe):
            def product(out, weight, hi, lo, first, last):
                nc.tensor.matmul(out, weight[0], hi, start=first, stop=False)
                nc.tensor.matmul(out, weight[0], lo, start=False, stop=False)
                return nc.tensor.matmul(out, weight[1], hi, start=False, stop=last)

            def tile(s, c):
                return w_hi[:, s, c * P:(c + 1) * P], w_lo[:, s, c * P:(c + 1) * P]

            def up(s, b, t):
                pe.wait_ge(w_ready, (b // NT) * NF + (s + 1))
                if s == 0:
                    pe.wait_ge(x_ready, t + 1)
                for ps, read, done, c0 in ((g_ps, silu_done, g_done, 0), (u_ps, h_done, u_done, K)):
                    if s >= 2 or not_first(b):
                        pe.wait_ge(read, b * NF + (s - 1))
                    for k in range(K):
                        col = t * XB + k * TB
                        last = product(ps[:, s % 2, :], tile(s, c0 + k), x_hi[:, bass.ds(col, TB)],
                                       x_lo[:, bass.ds(col, TB)], k == 0, k == K - 1)
                    last.then_inc(done, 1)

            def down(s, b):
                pe.wait_ge(h_lo_done, b * NF + (s + 1))
                if s == 0 and not_first(b):
                    pe.wait_ge(scaled_done, b)
                for d in range(K):
                    last = product(down_ps[:, d, :], tile(s, 2 * K + d), h_hi[:, s % 2, :], h_lo[:, s % 2, :],
                                   s == 0, s == NF - 1)
                last.then_inc(down_done, 1)

            def rest(b, t):
                for s in range(1, NF):
                    up(s, b, t)
                    down(s - 1, b)

            def whole(b):
                rest(b, b % NT)
                up(0, b + 1, (b + 1) % NT)
                down(NF - 1, b)

            up(0, 0, 0)
            whole(0)
            with pe.Fori(1, NB - 1) as b:
                whole(b)
            rest(NB - 1, NT - 1)
            down(NF - 1, NB - 1)

        @block.scalar
        def _(act):
            def step(s, b):
                early = s < 2 and not not_first(b)
                act.wait_ge(g_done, b * NF + (s + 1))
                if not early:
                    act.wait_ge(h_lo_done, b * NF + (s - 1))
                nc.scalar.activation(h[:, s % 2, :], g_ps[:, s % 2, :], ACT.Silu).then_inc(silu_done, 1)
                act.wait_ge(h_done, b * NF + (s + 1))
                if not early:
                    act.wait_ge(down_done, b * NF + (s - 1))
                nc.scalar.copy(h_hi[:, s % 2, :], h[:, s % 2, :]).then_inc(h_hi_done, 1)

            def rest(b):
                for s in range(1, NF):
                    step(s, b)

            step(0, 0)
            rest(0)
            with act.Fori(1, NB) as b:
                step(0, b)
                rest(b)

        @block.vector
        def _(dve):
            def step(s, b):
                dve.wait_ge(u_done, b * NF + (s + 1))
                dve.wait_ge(silu_done, b * NF + (s + 1))
                nc.vector.tensor_tensor(h[:, s % 2, :], u_ps[:, s % 2, :], h[:, s % 2, :],
                                        ALU.mult).then_inc(h_done, 1)
                dve.wait_ge(h_hi_done, b * NF + (s + 1))
                nc.vector.tensor_tensor(h_lo[:, s % 2, :], h[:, s % 2, :], h_hi[:, s % 2, :].bitcast(F32),
                                        ALU.subtract).then_inc(h_lo_done, 1)

            def finish(b, t):
                dve.wait_ge(down_done, b * NF + NF)
                c = coef[:, bass.ds(b * BPB, BPB)]
                c = bass.AP(c.tensor, c.offset, [c.ap[0], [0, K], c.ap[1], [0, SEQ]])
                split = "p (k b n) -> p k b n"
                nc.vector.tensor_tensor(scaled[:].rearrange(split, k=K, b=BPB),
                                        down_ps[:].rearrange("p k (b n) -> p k b n", b=BPB), c,
                                        ALU.mult).then_inc(scaled_done, 1)
                acc = out_acc[:, bass.ds(t * XB, XB)]
                dve.wait_ge(scaled_done, b + 1)
                nc.vector.tensor_tensor(acc, acc, scaled[:], ALU.add).then_inc(acc_done, 1)

            dve.wait_ge(gates_landed, 32)
            shared = coef[:, (NE - 1) * BATCH:]
            nc.vector.tensor_scalar(one_minus[:], shared, -1.0, 1.0, ALU.mult, ALU.add).then_inc(gates_step, 1)
            dve.wait_ge(gates_step, 1)
            for e in range(NE - 1):
                last = nc.vector.tensor_tensor(coef[:, e * BATCH:(e + 1) * BATCH], gates[:, :, e], one_minus[:],
                                               ALU.mult)
            last.then_inc(coef_ready, 1)
            step(0, 0)
            dve.wait_ge(coef_ready, 1)
            with dve.Fori(0, NB - 1) as b:
                for s in range(1, NF):
                    step(s, b)
                step(0, b + 1)
                finish(b, b % NT)
            for s in range(1, NF):
                step(s, NB - 1)
            finish(NB - 1, NT - 1)


def kernel(x, fside_Bx8_0, condB_sharedgateprob, L0_cond_Wg, L0_cond_Wu, L0_cond_Wd, L0_cond_Sg, L0_cond_Su,
           L0_cond_Sd):
    import numpy as np
    import concourse.bacc as bacc
    from concourse.bass_utils import run_bass_kernel_spmd

    x, gating, shared, wg, wu, wd, sg, su, sd = (np.asarray(a) for a in (
        x, fside_Bx8_0, condB_sharedgateprob, L0_cond_Wg, L0_cond_Wu, L0_cond_Wd, L0_cond_Sg, L0_cond_Su,
        L0_cond_Sd))
    D, F = sg.shape
    K, NF, NE = D // P, F // P, wg.shape[0] + 1
    NT = x.size // D // TB
    xt = np.ascontiguousarray(x.reshape(NT, TB, K, P).transpose(0, 3, 2, 1))

    def columns(w, s):
        w = np.concatenate([w, s[None]]).reshape(NE, K, P, NF, P)
        return w.transpose(0, 3, 2, 1, 4)

    down = np.concatenate([wd, sd[None]]).reshape(NE, NF, P, K, P)
    w = np.concatenate([columns(wg, sg), columns(wu, su), down], axis=3)
    w = np.ascontiguousarray(w.reshape(NE, NF, P, 3 * K * P))

    nc = bacc.Bacc("TRN2", target_bir_lowering=False, num_devices=1)
    arrays = {"x_t": xt, "gating": np.ascontiguousarray(gating), "shared": np.ascontiguousarray(shared), "w": w}
    aps = [nc.dram_tensor(n, a.shape, F32, kind="ExternalInput").ap() for n, a in arrays.items()]
    out = nc.dram_tensor("out", xt.shape, F32, kind="ExternalOutput").ap()
    moe_program(nc, *aps, out)
    r = run_bass_kernel_spmd(nc, [arrays], core_ids=[0])
    got = r.results[0]["out"]
    return got.transpose(0, 3, 2, 1).reshape(x.shape)
```

```python
from contextlib import ExitStack

import concourse.bass as bass
from concourse import mybir

F32 = mybir.dt.float32
F32R = mybir.dt.float32r
ALU = mybir.AluOpType
ACT = mybir.ActivationFunctionType

P = 128
TB = 512
WARM = 7


def not_first(b):
    return not (isinstance(b, int) and b == 0)


def moe_program(nc, x_dram, gating_dram, shared_dram, w_dram, out_dram):
    NT, _, K, _ = x_dram.shape
    NE, NF, _, SLICE = w_dram.shape
    BATCH = shared_dram.shape[0]
    SEQ = NT * TB // BATCH
    BPB = TB // SEQ
    NB = NE * NT
    D = K * P

    with ExitStack() as ctx:
        def sb(name, shape, dt=F32):
            return ctx.enter_context(nc.sbuf_tensor(name, shape, dt))

        def sem(name):
            return ctx.enter_context(nc.semaphore(name))

        out_acc = sb("out_acc", [P, NT * K * TB])
        x_hi = sb("x_hi", [P, NT * K * TB], F32R)
        x_lo = sb("x_lo", [P, NT * K * TB], F32R)
        w_stage = sb("w_stage", [P, NF, SLICE])
        w_hi = sb("w_hi", [P, NF, SLICE], F32R)
        w_lo = sb("w_lo", [P, NF, SLICE], F32R)
        h = sb("h", [P, 2, TB])
        h_hi = sb("h_hi", [P, 2, TB], F32R)
        h_lo = sb("h_lo", [P, 2, TB], F32R)
        scaled = sb("scaled", [P, K * TB])
        zero = sb("zero", [P, 1])
        silu_of_zero = sb("silu_of_zero", [P, 1])
        warm = sb("warm", [P, TB], F32R)
        gates = sb("gates", [P, BATCH, NE - 1])
        coef = sb("coef", [P, NE * BATCH])
        one_minus = sb("one_minus", [P, BATCH])

        g_ps = ctx.enter_context(nc.psum_tensor("g_ps", [P, 2, TB], F32))
        u_ps = ctx.enter_context(nc.psum_tensor("u_ps", [P, 2, TB], F32))
        down_ps = ctx.enter_context(nc.psum_tensor("down_ps", [P, K, TB], F32))

        x0_landed = [sem(f"x0_landed{k}") for k in range(K)]
        w0_gate_landed = sem("w0_gate_landed")
        w0_rest_landed = sem("w0_rest_landed")
        x_landed = [sem(f"x_landed{t}") for t in range(1, NT)]
        w_landed = [sem(f"w_landed{s}") for s in range(NF)]
        gates_landed = sem("gates_landed")
        gates_step = sem("gates_step")
        coef_ready = sem("coef_ready")
        zero_set = sem("zero_set")
        warm_set = sem("warm_set")
        x0_hi_done = sem("x0_hi_done")
        x0_ready = sem("x0_ready")
        w0_gate_hi_done = sem("w0_gate_hi_done")
        w0_gate_ready = sem("w0_gate_ready")
        w0_rest_hi_done = sem("w0_rest_hi_done")
        x_hi_done = sem("x_hi_done")
        x_ready = sem("x_ready")
        w_hi_done = sem("w_hi_done")
        w_ready = sem("w_ready")
        g_done = sem("g_done")
        u_done = sem("u_done")
        silu_done = sem("silu_done")
        h_done = sem("h_done")
        h_hi_done = sem("h_hi_done")
        h_lo_done = sem("h_lo_done")
        down_done = sem("down_done")
        scaled_done = sem("scaled_done")
        acc_done = sem("acc_done")
        last_down = sem("last_down")
        last_scaled = sem("last_scaled")
        last_acc = sem("last_acc")
        stored = sem("stored")

        block = ctx.enter_context(nc.Block())
        XB = K * TB
        GATE = K * P

        @block.sync
        def _(sp):
            def load_x(t):
                sp.dma_start(out_acc[:, t * XB:(t + 1) * XB],
                             x_dram[t].rearrange("p k n -> p (k n)")).then_inc(x_landed[t - 1], 16)

            sp.dma_start(w_stage[:, 0, :GATE], w_dram[0, 0][:, :GATE]).then_inc(w0_gate_landed, 16)
            sp.dma_start(out_acc[:, TB:XB], x_dram[0][:, 1:].rearrange("p k n -> p (k n)")).then_inc(x0_landed[1], 16)
            for s in range(1, NF):
                sp.dma_start(w_stage[:, s, :], w_dram[0, s]).then_inc(w_landed[s], 16)
            sp.dma_start(gates[:].rearrange("p b e -> p (b e)"),
                         gating_dram.rearrange("b e -> (b e)").partition_broadcast(P)).then_inc(gates_landed, 16)
            sp.dma_start(coef[:, (NE - 1) * BATCH:], shared_dram.partition_broadcast(P)).then_inc(gates_landed, 16)
            for t in range(1, NT):
                load_x(t)
            with sp.Fori(1, NE) as e:
                for s in range(NF):
                    sp.wait_ge(w_ready, (e - 1) * NF + (s + 1))
                    sp.dma_start(w_stage[:, s, :],
                                 w_dram[bass.ds(e, 1), s].rearrange("a p n -> (a p) n")).then_inc(w_landed[s], 16)
            for t in range(NT - 1):
                sp.wait_ge(acc_done, NB - NT + t + 1)
                sp.dma_start(out_dram[t].rearrange("p k n -> p (k n)"),
                             out_acc[:, t * XB:(t + 1) * XB]).then_inc(stored, 16)
            for d in range(K):
                sp.wait_ge(last_acc, d + 1)
                c = (NT - 1) * XB + d * TB
                sp.dma_start(out_dram[NT - 1][:, d], out_acc[:, c:c + TB]).then_inc(stored, 16)
            sp.wait_ge(stored, 16 * (NT - 1 + K))

        @block.gpsimd
        def _(pool):
            def split_x(t):
                c = slice(t * XB, (t + 1) * XB)
                pool.wait_ge(x_landed[t - 1], 16)
                nc.gpsimd.tensor_copy(x_hi[:, c], out_acc[:, c]).then_inc(x_hi_done, 1)
                pool.wait_ge(x_hi_done, t)
                nc.gpsimd.tensor_tensor(x_lo[:, c], out_acc[:, c], x_hi[:, c].bitcast(F32),
                                        ALU.subtract).then_inc(x_ready, 1)

            def split_slice(s, done):
                nc.gpsimd.tensor_tensor(w_hi[:, s, :], w_stage[:, s, :], zero[:, 0:1].to_broadcast([P, SLICE]),
                                        ALU.subtract).then_inc(w_hi_done, 1)
                pool.wait_ge(w_hi_done, done + 1)
                nc.gpsimd.tensor_tensor(w_lo[:, s, :], w_stage[:, s, :], w_hi[:, s, :].bitcast(F32),
                                        ALU.subtract).then_inc(w_ready, 1)

            nc.gpsimd.memset(zero[:], 0.0).then_inc(zero_set, 1)
            for s in range(1, NF):
                pool.wait_ge(w_landed[s], 16)
                nc.gpsimd.tensor_copy(w_hi[:, s, :], w_stage[:, s, :]).then_inc(w_hi_done, 1)
            pool.wait_ge(x_ready, 1)
            for t in range(1, NT):
                split_x(t)
            pool.wait_ge(zero_set, 1)
            with pool.Fori(1, NE) as e:
                for s in range(NF):
                    pool.wait_ge(w_landed[s], e * 16 + (16 if s else 0))
                    pool.wait_ge(down_done, e * (NT * NF) + (s + 1 - NF))
                    split_slice(s, e * NF + (s - 1))

        @block.tensor
        def _(pe):
            def product(out, weight, hi, lo, first, last):
                nc.tensor.matmul(out, weight[0], hi, start=first, stop=False)
                nc.tensor.matmul(out, weight[0], lo, start=False, stop=False)
                return nc.tensor.matmul(out, weight[1], hi, start=False, stop=last)

            def tile(s, c):
                return w_hi[:, s, c * P:(c + 1) * P], w_lo[:, s, c * P:(c + 1) * P]

            def up_product(ps, s, c0, k, t):
                x = bass.ds(t * XB + k * TB, TB)
                return product(ps[:, s % 2, :], tile(s, c0 + k), x_hi[:, x], x_lo[:, x], k == 0, k == K - 1)

            def up(s, b, t):
                pe.wait_ge(w_ready, (b // NT) * NF + (s + 1))
                if s == 0:
                    pe.wait_ge(x_ready, t + 1)
                for ps, read, done, c0 in ((g_ps, silu_done, g_done, 0), (u_ps, h_done, u_done, K)):
                    if s >= 2 or not_first(b):
                        pe.wait_ge(read, b * NF + (s - 1))
                    for k in range(K):
                        last = up_product(ps, s, c0, k, t)
                    last.then_inc(done, 1)

            def first_up():
                pe.wait_ge(w0_gate_ready, 1)
                for k in range(K):
                    if k < K - 1:
                        pe.wait_ge(x0_ready, k + 1)
                    else:
                        pe.wait_ge(x_ready, 1)
                    last = up_product(g_ps, 0, 0, k, 0)
                last.then_inc(g_done, 1)
                pe.wait_ge(w_ready, 1)
                for k in range(K):
                    last = up_product(u_ps, 0, K, k, 0)
                last.then_inc(u_done, 1)

            def down(s, b, parts=False):
                pe.wait_ge(h_lo_done, b * NF + (s + 1))
                if s == 0 and not_first(b):
                    pe.wait_ge(scaled_done, b)
                for d in range(K):
                    last = product(down_ps[:, d, :], tile(s, 2 * K + d), h_hi[:, s % 2, :], h_lo[:, s % 2, :],
                                   s == 0, s == NF - 1)
                    if parts:
                        last.then_inc(last_down, 1)
                if not parts:
                    last.then_inc(down_done, 1)

            def rest(b, t):
                for s in range(1, NF):
                    up(s, b, t)
                    down(s - 1, b)

            def block_of(b):
                rest(b, b % NT)
                up(0, b + 1, (b + 1) % NT)
                down(NF - 1, b)

            pe.wait_ge(warm_set, 1)
            for _ in range(WARM):
                nc.tensor.matmul(down_ps[:, 0, :], warm[:, :P], warm[:], start=True, stop=True)
            first_up()
            block_of(0)
            with pe.Fori(1, NB - 1) as b:
                block_of(b)
            rest(NB - 1, NT - 1)
            down(NF - 1, NB - 1, parts=True)

        @block.scalar
        def _(act):
            def step(s, b):
                early = s < 2 and not not_first(b)
                act.wait_ge(g_done, b * NF + (s + 1))
                if not early:
                    act.wait_ge(h_lo_done, b * NF + (s - 1))
                nc.scalar.activation(h[:, s % 2, :], g_ps[:, s % 2, :], ACT.Silu).then_inc(silu_done, 1)
                act.wait_ge(h_done, b * NF + (s + 1))
                if not early:
                    act.wait_ge(down_done, b * NF + (s - 1))
                nc.scalar.copy(h_hi[:, s % 2, :], h[:, s % 2, :]).then_inc(h_hi_done, 1)

            def rest(b):
                for s in range(1, NF):
                    step(s, b)

            act.dma_start(out_acc[:, :TB], x_dram[0][:, 0]).then_inc(x0_landed[0], 16)
            act.dma_start(w_stage[:, 0, GATE:], w_dram[0, 0][:, GATE:]).then_inc(w0_rest_landed, 16)
            act.wait_ge(warm_set, 1)
            nc.scalar.activation(silu_of_zero[:], warm[:, 0:1].bitcast(F32), ACT.Silu)
            for k in range(K):
                act.wait_ge(x0_landed[k], 16)
                nc.scalar.copy(x_hi[:, k * TB:(k + 1) * TB], out_acc[:, k * TB:(k + 1) * TB]).then_inc(x0_hi_done, 1)
            act.wait_ge(w0_rest_landed, 16)
            nc.scalar.copy(w_hi[:, 0, GATE:], w_stage[:, 0, GATE:]).then_inc(w0_rest_hi_done, 1)
            step(0, 0)
            rest(0)
            with act.Fori(1, NB) as b:
                step(0, b)
                rest(b)

        @block.vector
        def _(dve):
            def step(s, b):
                dve.wait_ge(u_done, b * NF + (s + 1))
                dve.wait_ge(silu_done, b * NF + (s + 1))
                nc.vector.tensor_tensor(h[:, s % 2, :], u_ps[:, s % 2, :], h[:, s % 2, :],
                                        ALU.mult).then_inc(h_done, 1)
                dve.wait_ge(h_hi_done, b * NF + (s + 1))
                nc.vector.tensor_tensor(h_lo[:, s % 2, :], h[:, s % 2, :], h_hi[:, s % 2, :].bitcast(F32),
                                        ALU.subtract).then_inc(h_lo_done, 1)

            def finish(b, t):
                dve.wait_ge(down_done, b * NF + NF)
                c = coef[:, bass.ds(b * BPB, BPB)]
                c = bass.AP(c.tensor, c.offset, [c.ap[0], [0, K], c.ap[1], [0, SEQ]])
                split = "p (k b n) -> p k b n"
                nc.vector.tensor_tensor(scaled[:].rearrange(split, k=K, b=BPB),
                                        down_ps[:].rearrange("p k (b n) -> p k b n", b=BPB), c,
                                        ALU.mult).then_inc(scaled_done, 1)
                acc = out_acc[:, bass.ds(t * XB, XB)]
                dve.wait_ge(scaled_done, b + 1)
                nc.vector.tensor_tensor(acc, acc, scaled[:], ALU.add).then_inc(acc_done, 1)

            def lo(dst, whole, hi, done):
                nc.vector.tensor_tensor(dst, whole, hi.bitcast(F32), ALU.subtract).then_inc(done, 1)

            def slice_lo(s):
                dve.wait_ge(w_hi_done, s)
                lo(w_lo[:, s, :], w_stage[:, s, :], w_hi[:, s, :], w_ready)

            def coefficients():
                dve.wait_ge(gates_landed, 32)
                shared = coef[:, (NE - 1) * BATCH:]
                nc.vector.tensor_scalar(one_minus[:], shared, -1.0, 1.0, ALU.mult, ALU.add).then_inc(gates_step, 1)
                dve.wait_ge(gates_step, 1)
                for e in range(NE - 1):
                    last = nc.vector.tensor_tensor(coef[:, e * BATCH:(e + 1) * BATCH], gates[:, :, e], one_minus[:],
                                                   ALU.mult)
                last.then_inc(coef_ready, 1)

            nc.vector.memset(warm[:].bitcast(F32), 0.0).then_inc(warm_set, 1)
            dve.wait_ge(w0_gate_landed, 16)
            nc.vector.tensor_copy(w_hi[:, 0, :GATE], w_stage[:, 0, :GATE]).then_inc(w0_gate_hi_done, 1)
            dve.wait_ge(w0_gate_hi_done, 1)
            lo(w_lo[:, 0, :GATE], w_stage[:, 0, :GATE], w_hi[:, 0, :GATE], w0_gate_ready)
            for k in range(K):
                dve.wait_ge(x0_hi_done, k + 1)
                c = slice(k * TB, (k + 1) * TB)
                lo(x_lo[:, c], out_acc[:, c], x_hi[:, c], x0_ready if k < K - 1 else x_ready)
            dve.wait_ge(w0_rest_hi_done, 1)
            lo(w_lo[:, 0, GATE:], w_stage[:, 0, GATE:], w_hi[:, 0, GATE:], w_ready)

            for s in range(NF):
                if s + 1 < NF:
                    slice_lo(s + 1)
                step(s, 0)
            coefficients()
            step(0, 1)
            dve.wait_ge(coef_ready, 1)
            finish(0, 0)
            with dve.Fori(1, NB - 1) as b:
                for s in range(1, NF):
                    step(s, b)
                step(0, b + 1)
                finish(b, b % NT)
            for s in range(1, NF):
                step(s, NB - 1)
            for d in range(K):
                dve.wait_ge(last_down, d + 1)
                part = scaled[:, d * TB:(d + 1) * TB]
                c = coef[:, (NB - 1) * BPB:]
                c = bass.AP(c.tensor, c.offset, [c.ap[0], c.ap[1], [0, SEQ]])
                split = "p (b n) -> p b n"
                nc.vector.tensor_tensor(part.rearrange(split, b=BPB), down_ps[:, d, :].rearrange(split, b=BPB), c,
                                        ALU.mult).then_inc(last_scaled, 1)
                acc = out_acc[:, (NT - 1) * XB + d * TB:(NT - 1) * XB + (d + 1) * TB]
                dve.wait_ge(last_scaled, d + 1)
                nc.vector.tensor_tensor(acc, acc, part, ALU.add).then_inc(last_acc, 1)


def kernel(x, fside_Bx8_0, condB_sharedgateprob, L0_cond_Wg, L0_cond_Wu, L0_cond_Wd, L0_cond_Sg, L0_cond_Su,
           L0_cond_Sd):
    import numpy as np
    import concourse.bacc as bacc
    from concourse.bass_utils import run_bass_kernel_spmd

    x, gating, shared, wg, wu, wd, sg, su, sd = (np.asarray(a) for a in (
        x, fside_Bx8_0, condB_sharedgateprob, L0_cond_Wg, L0_cond_Wu, L0_cond_Wd, L0_cond_Sg, L0_cond_Su,
        L0_cond_Sd))
    D, F = sg.shape
    K, NF, NE = D // P, F // P, wg.shape[0] + 1
    NT = x.size // D // TB
    xt = np.ascontiguousarray(x.reshape(NT, TB, K, P).transpose(0, 3, 2, 1))

    def columns(w, s):
        w = np.concatenate([w, s[None]]).reshape(NE, K, P, NF, P)
        return w.transpose(0, 3, 2, 1, 4)

    down = np.concatenate([wd, sd[None]]).reshape(NE, NF, P, K, P)
    w = np.concatenate([columns(wg, sg), columns(wu, su), down], axis=3)
    w = np.ascontiguousarray(w.reshape(NE, NF, P, 3 * K * P))

    nc = bacc.Bacc("TRN2", target_bir_lowering=False, num_devices=1)
    arrays = {"x_t": xt, "gating": np.ascontiguousarray(gating), "shared": np.ascontiguousarray(shared), "w": w}
    aps = [nc.dram_tensor(n, a.shape, F32, kind="ExternalInput").ap() for n, a in arrays.items()]
    out = nc.dram_tensor("out", xt.shape, F32, kind="ExternalOutput").ap()
    moe_program(nc, *aps, out)
    r = run_bass_kernel_spmd(nc, [arrays], core_ids=[0])
    got = r.results[0]["out"]
    return got.transpose(0, 3, 2, 1).reshape(x.shape)
```

```python
from contextlib import ExitStack

import concourse.bass as bass
from concourse import mybir

F32 = mybir.dt.float32
F32R = mybir.dt.float32r
ALU = mybir.AluOpType
ACT = mybir.ActivationFunctionType

P = 128
TB = 512
WARM = 9


def not_first(b):
    return not (isinstance(b, int) and b == 0)


def moe_program(nc, x_dram, gating_dram, shared_dram, w_dram, out_dram):
    NT, _, K, _ = x_dram.shape
    NE, NF, _, SLICE = w_dram.shape
    BATCH = shared_dram.shape[0]
    SEQ = NT * TB // BATCH
    BPB = TB // SEQ
    NB = NE * NT
    D = K * P

    with ExitStack() as ctx:
        def sb(name, shape, dt=F32):
            return ctx.enter_context(nc.sbuf_tensor(name, shape, dt))

        def sem(name):
            return ctx.enter_context(nc.semaphore(name))

        out_acc = sb("out_acc", [P, NT * K * TB])
        x_hi = sb("x_hi", [P, NT * K * TB], F32R)
        x_lo = sb("x_lo", [P, NT * K * TB], F32R)
        w_stage = sb("w_stage", [P, NF, SLICE])
        w_hi = sb("w_hi", [P, NF, SLICE], F32R)
        w_lo = sb("w_lo", [P, NF, SLICE], F32R)
        h = sb("h", [P, 2, TB])
        h_hi = sb("h_hi", [P, 2, TB], F32R)
        h_lo = sb("h_lo", [P, 2, TB], F32R)
        scaled = sb("scaled", [P, K * TB])
        zero = sb("zero", [P, 1])
        silu_of_zero = sb("silu_of_zero", [P, 1])
        warm = sb("warm", [P, TB], F32R)
        gates = sb("gates", [P, BATCH, NE - 1])
        coef = sb("coef", [P, NE * BATCH])
        one_minus = sb("one_minus", [P, BATCH])

        g_ps = ctx.enter_context(nc.psum_tensor("g_ps", [P, 2, TB], F32))
        u_ps = ctx.enter_context(nc.psum_tensor("u_ps", [P, 2, TB], F32))
        down_ps = ctx.enter_context(nc.psum_tensor("down_ps", [P, K, TB], F32))

        x0_landed = [sem(f"x0_landed{k}") for k in range(K)]
        w0_gate_landed = sem("w0_gate_landed")
        w0_rest_landed = sem("w0_rest_landed")
        x_landed = [sem(f"x_landed{t}") for t in range(1, NT)]
        w_landed = [sem(f"w_landed{s}") for s in range(NF)]
        gates_landed = sem("gates_landed")
        gates_step = sem("gates_step")
        coef_ready = sem("coef_ready")
        zero_set = sem("zero_set")
        warm_set = sem("warm_set")
        x0_hi_done = sem("x0_hi_done")
        x0_ready = sem("x0_ready")
        w0_gate_hi_done = sem("w0_gate_hi_done")
        w0_gate_ready = sem("w0_gate_ready")
        w0_rest_hi_done = sem("w0_rest_hi_done")
        w1_hi_done = sem("w1_hi_done")
        x_hi_done = sem("x_hi_done")
        x_ready = sem("x_ready")
        w_hi_done = sem("w_hi_done")
        w_ready = sem("w_ready")
        g_done = sem("g_done")
        u_done = sem("u_done")
        silu_done = sem("silu_done")
        h_done = sem("h_done")
        h_hi_done = sem("h_hi_done")
        h_lo_done = sem("h_lo_done")
        down_done = sem("down_done")
        scaled_done = sem("scaled_done")
        acc_done = sem("acc_done")
        last_h = sem("last_h")
        last_h_hi = sem("last_h_hi")
        last_h_lo = sem("last_h_lo")
        last_down = sem("last_down")
        last_scaled = sem("last_scaled")
        last_acc = sem("last_acc")
        stored = sem("stored")

        block = ctx.enter_context(nc.Block())
        XB = K * TB
        GATE = K * P
        HALVES = [slice(0, TB // 2), slice(TB // 2, TB)]

        @block.sync
        def _(sp):
            def load_x(t):
                sp.dma_start(out_acc[:, t * XB:(t + 1) * XB],
                             x_dram[t].rearrange("p k n -> p (k n)")).then_inc(x_landed[t - 1], 16)

            sp.dma_start(w_stage[:, 0, :GATE], w_dram[0, 0][:, :GATE]).then_inc(w0_gate_landed, 16)
            sp.dma_start(out_acc[:, TB:XB], x_dram[0][:, 1:].rearrange("p k n -> p (k n)")).then_inc(x0_landed[1], 16)
            for s in range(1, NF):
                sp.dma_start(w_stage[:, s, :], w_dram[0, s]).then_inc(w_landed[s], 16)
            sp.dma_start(gates[:].rearrange("p b e -> p (b e)"),
                         gating_dram.rearrange("b e -> (b e)").partition_broadcast(P)).then_inc(gates_landed, 16)
            sp.dma_start(coef[:, (NE - 1) * BATCH:], shared_dram.partition_broadcast(P)).then_inc(gates_landed, 16)
            for t in range(1, NT):
                load_x(t)
            with sp.Fori(1, NE) as e:
                for s in range(NF):
                    sp.wait_ge(w_ready, (e - 1) * NF + (s + 1))
                    sp.dma_start(w_stage[:, s, :],
                                 w_dram[bass.ds(e, 1), s].rearrange("a p n -> (a p) n")).then_inc(w_landed[s], 16)
            for t in range(NT - 1):
                sp.wait_ge(acc_done, NB - NT + t + 1)
                sp.dma_start(out_dram[t].rearrange("p k n -> p (k n)"),
                             out_acc[:, t * XB:(t + 1) * XB]).then_inc(stored, 16)
            for d in range(K):
                sp.wait_ge(last_acc, d + 1)
                c = (NT - 1) * XB + d * TB
                sp.dma_start(out_dram[NT - 1][:, d], out_acc[:, c:c + TB]).then_inc(stored, 16)
            sp.wait_ge(stored, 16 * (NT - 1 + K))

        @block.gpsimd
        def _(pool):
            def split_x(t):
                c = slice(t * XB, (t + 1) * XB)
                pool.wait_ge(x_landed[t - 1], 16)
                nc.gpsimd.tensor_copy(x_hi[:, c], out_acc[:, c]).then_inc(x_hi_done, 1)
                pool.wait_ge(x_hi_done, t)
                nc.gpsimd.tensor_tensor(x_lo[:, c], out_acc[:, c], x_hi[:, c].bitcast(F32),
                                        ALU.subtract).then_inc(x_ready, 1)

            def split_slice(s, done):
                nc.gpsimd.tensor_tensor(w_hi[:, s, :], w_stage[:, s, :], zero[:, 0:1].to_broadcast([P, SLICE]),
                                        ALU.subtract).then_inc(w_hi_done, 1)
                pool.wait_ge(w_hi_done, done + 1)
                nc.gpsimd.tensor_tensor(w_lo[:, s, :], w_stage[:, s, :], w_hi[:, s, :].bitcast(F32),
                                        ALU.subtract).then_inc(w_ready, 1)

            nc.gpsimd.memset(zero[:], 0.0).then_inc(zero_set, 1)
            for s in range(2, NF):
                pool.wait_ge(w_landed[s], 16)
                nc.gpsimd.tensor_copy(w_hi[:, s, :], w_stage[:, s, :]).then_inc(w_hi_done, 1)
            pool.wait_ge(x_ready, 1)
            for t in range(1, NT):
                split_x(t)
            pool.wait_ge(zero_set, 1)
            with pool.Fori(1, NE) as e:
                for s in range(NF):
                    pool.wait_ge(w_landed[s], e * 16 + (16 if s else 0))
                    pool.wait_ge(down_done, e * (NT * NF) + (s + 1 - NF))
                    split_slice(s, e * NF + (s - 2))

        @block.tensor
        def _(pe):
            def product(out, weight, hi, lo, first, last):
                nc.tensor.matmul(out, weight[0], hi, start=first, stop=False)
                nc.tensor.matmul(out, weight[0], lo, start=False, stop=False)
                return nc.tensor.matmul(out, weight[1], hi, start=False, stop=last)

            def tile(s, c):
                return w_hi[:, s, c * P:(c + 1) * P], w_lo[:, s, c * P:(c + 1) * P]

            def up(s, b, t):
                pe.wait_ge(w_ready, (b // NT) * NF + (s + 1))
                if s == 0:
                    pe.wait_ge(x_ready, t + 1)
                for ps, read, done, c0 in ((g_ps, silu_done, g_done, 0), (u_ps, h_done, u_done, K)):
                    if s >= 2 or not_first(b):
                        pe.wait_ge(read, b * NF + (s - 1))
                    for k in range(K):
                        x = bass.ds(t * XB + k * TB, TB)
                        last = product(ps[:, s % 2, :], tile(s, c0 + k), x_hi[:, x], x_lo[:, x], k == 0, k == K - 1)
                    last.then_inc(done, 1)

            def first_up():
                x = [slice(k * TB, (k + 1) * TB) for k in range(K)]
                pe.wait_ge(w0_gate_ready, 1)
                for k in range(K):
                    pe.wait_ge(x0_hi_done, k + 1)
                    nc.tensor.matmul(g_ps[:, 0, :], tile(0, k)[0], x_hi[:, x[k]], start=(k == 0), stop=False)
                    nc.tensor.matmul(g_ps[:, 0, :], tile(0, k)[1], x_hi[:, x[k]], start=False, stop=False)
                for k in range(K):
                    if k < K - 1:
                        pe.wait_ge(x0_ready, k + 1)
                    else:
                        pe.wait_ge(x_ready, 1)
                    last = nc.tensor.matmul(g_ps[:, 0, :], tile(0, k)[0], x_lo[:, x[k]], start=False, stop=(k == K - 1))
                last.then_inc(g_done, 1)
                pe.wait_ge(w0_rest_hi_done, 1)
                for k in range(K):
                    nc.tensor.matmul(u_ps[:, 0, :], tile(0, K + k)[0], x_hi[:, x[k]], start=(k == 0), stop=False)
                    nc.tensor.matmul(u_ps[:, 0, :], tile(0, K + k)[0], x_lo[:, x[k]], start=False, stop=False)
                pe.wait_ge(w_ready, 1)
                for k in range(K):
                    last = nc.tensor.matmul(u_ps[:, 0, :], tile(0, K + k)[1], x_hi[:, x[k]], start=False,
                                            stop=(k == K - 1))
                last.then_inc(u_done, 1)

            def down(s, b):
                pe.wait_ge(h_lo_done, b * NF + (s + 1))
                if s == 0 and not_first(b):
                    pe.wait_ge(scaled_done, b)
                for d in range(K):
                    last = product(down_ps[:, d, :], tile(s, 2 * K + d), h_hi[:, s % 2, :], h_lo[:, s % 2, :],
                                   s == 0, s == NF - 1)
                last.then_inc(down_done, 1)

            def last_step_down():
                s = NF - 1
                for half, c in enumerate(HALVES):
                    pe.wait_ge(last_h_lo, half + 1)
                    for d in range(K):
                        last = product(down_ps[:, d, c], tile(s, 2 * K + d), h_hi[:, s % 2, c], h_lo[:, s % 2, c],
                                       False, half == len(HALVES) - 1)
                        if half == len(HALVES) - 1:
                            last.then_inc(last_down, 1)

            def rest(b, t):
                for s in range(1, NF):
                    up(s, b, t)
                    down(s - 1, b)

            def block_of(b):
                rest(b, b % NT)
                up(0, b + 1, (b + 1) % NT)
                down(NF - 1, b)

            pe.wait_ge(warm_set, 1)
            for _ in range(WARM):
                nc.tensor.matmul(down_ps[:, 0, :], warm[:, :P], warm[:], start=True, stop=True)
            first_up()
            block_of(0)
            with pe.Fori(1, NB - 1) as b:
                block_of(b)
            rest(NB - 1, NT - 1)
            last_step_down()

        @block.scalar
        def _(act):
            def step(s, b):
                early = s < 2 and not not_first(b)
                act.wait_ge(g_done, b * NF + (s + 1))
                if not early:
                    act.wait_ge(h_lo_done, b * NF + (s - 1))
                nc.scalar.activation(h[:, s % 2, :], g_ps[:, s % 2, :], ACT.Silu).then_inc(silu_done, 1)
                act.wait_ge(h_done, b * NF + (s + 1))
                if not early:
                    act.wait_ge(down_done, b * NF + (s - 1))
                nc.scalar.copy(h_hi[:, s % 2, :], h[:, s % 2, :]).then_inc(h_hi_done, 1)

            def rest(b):
                for s in range(1, NF):
                    step(s, b)

            act.dma_start(out_acc[:, :TB], x_dram[0][:, 0]).then_inc(x0_landed[0], 16)
            act.dma_start(w_stage[:, 0, GATE:], w_dram[0, 0][:, GATE:]).then_inc(w0_rest_landed, 16)
            act.wait_ge(warm_set, 1)
            nc.scalar.activation(silu_of_zero[:], warm[:, 0:1].bitcast(F32), ACT.Silu)
            for k in range(K):
                act.wait_ge(x0_landed[k], 16)
                nc.scalar.copy(x_hi[:, k * TB:(k + 1) * TB], out_acc[:, k * TB:(k + 1) * TB]).then_inc(x0_hi_done, 1)
            act.wait_ge(w0_rest_landed, 16)
            nc.scalar.copy(w_hi[:, 0, GATE:], w_stage[:, 0, GATE:]).then_inc(w0_rest_hi_done, 1)
            act.wait_ge(w_landed[1], 16)
            nc.scalar.copy(w_hi[:, 1, :], w_stage[:, 1, :]).then_inc(w1_hi_done, 1)
            step(0, 0)
            rest(0)
            with act.Fori(1, NB - 1) as b:
                step(0, b)
                rest(b)
            for s in range(NF - 1):
                step(s, NB - 1)
            s = NF - 1
            act.wait_ge(g_done, NB * NF)
            act.wait_ge(h_lo_done, NB * NF - 2)
            nc.scalar.activation(h[:, s % 2, :], g_ps[:, s % 2, :], ACT.Silu).then_inc(silu_done, 1)
            act.wait_ge(down_done, NB * NF - 2)
            for half, c in enumerate(HALVES):
                act.wait_ge(last_h, half + 1)
                nc.scalar.copy(h_hi[:, s % 2, c], h[:, s % 2, c]).then_inc(last_h_hi, 1)

        @block.vector
        def _(dve):
            def step(s, b):
                dve.wait_ge(u_done, b * NF + (s + 1))
                dve.wait_ge(silu_done, b * NF + (s + 1))
                nc.vector.tensor_tensor(h[:, s % 2, :], u_ps[:, s % 2, :], h[:, s % 2, :],
                                        ALU.mult).then_inc(h_done, 1)
                dve.wait_ge(h_hi_done, b * NF + (s + 1))
                nc.vector.tensor_tensor(h_lo[:, s % 2, :], h[:, s % 2, :], h_hi[:, s % 2, :].bitcast(F32),
                                        ALU.subtract).then_inc(h_lo_done, 1)

            def finish(b, t):
                dve.wait_ge(down_done, b * NF + NF)
                c = coef[:, bass.ds(b * BPB, BPB)]
                c = bass.AP(c.tensor, c.offset, [c.ap[0], [0, K], c.ap[1], [0, SEQ]])
                split = "p (k b n) -> p k b n"
                nc.vector.tensor_tensor(scaled[:].rearrange(split, k=K, b=BPB),
                                        down_ps[:].rearrange("p k (b n) -> p k b n", b=BPB), c,
                                        ALU.mult).then_inc(scaled_done, 1)
                acc = out_acc[:, bass.ds(t * XB, XB)]
                dve.wait_ge(scaled_done, b + 1)
                nc.vector.tensor_tensor(acc, acc, scaled[:], ALU.add).then_inc(acc_done, 1)

            def lo(dst, whole, hi, done):
                nc.vector.tensor_tensor(dst, whole, hi.bitcast(F32), ALU.subtract).then_inc(done, 1)

            def slice_lo(s):
                if s == 1:
                    dve.wait_ge(w1_hi_done, 1)
                else:
                    dve.wait_ge(w_hi_done, s - 1)
                lo(w_lo[:, s, :], w_stage[:, s, :], w_hi[:, s, :], w_ready)

            def coefficients():
                dve.wait_ge(gates_landed, 32)
                shared = coef[:, (NE - 1) * BATCH:]
                nc.vector.tensor_scalar(one_minus[:], shared, -1.0, 1.0, ALU.mult, ALU.add).then_inc(gates_step, 1)
                dve.wait_ge(gates_step, 1)
                for e in range(NE - 1):
                    last = nc.vector.tensor_tensor(coef[:, e * BATCH:(e + 1) * BATCH], gates[:, :, e], one_minus[:],
                                                   ALU.mult)
                last.then_inc(coef_ready, 1)

            nc.vector.memset(warm[:].bitcast(F32), 0.0).then_inc(warm_set, 1)
            dve.wait_ge(w0_gate_landed, 16)
            nc.vector.tensor_copy(w_hi[:, 0, :GATE], w_stage[:, 0, :GATE]).then_inc(w0_gate_hi_done, 1)
            dve.wait_ge(w0_gate_hi_done, 1)
            lo(w_lo[:, 0, :GATE], w_stage[:, 0, :GATE], w_hi[:, 0, :GATE], w0_gate_ready)
            for k in range(K):
                dve.wait_ge(x0_hi_done, k + 1)
                c = slice(k * TB, (k + 1) * TB)
                lo(x_lo[:, c], out_acc[:, c], x_hi[:, c], x0_ready if k < K - 1 else x_ready)
            dve.wait_ge(w0_rest_hi_done, 1)
            lo(w_lo[:, 0, GATE:], w_stage[:, 0, GATE:], w_hi[:, 0, GATE:], w_ready)

            for s in range(NF):
                if s + 1 < NF:
                    slice_lo(s + 1)
                step(s, 0)
            coefficients()
            step(0, 1)
            dve.wait_ge(coef_ready, 1)
            finish(0, 0)
            with dve.Fori(1, NB - 1) as b:
                for s in range(1, NF):
                    step(s, b)
                step(0, b + 1)
                finish(b, b % NT)
            for s in range(1, NF - 1):
                step(s, NB - 1)
            s = NF - 1
            dve.wait_ge(u_done, NB * NF)
            dve.wait_ge(silu_done, NB * NF)
            for c in HALVES:
                nc.vector.tensor_tensor(h[:, s % 2, c], u_ps[:, s % 2, c], h[:, s % 2, c], ALU.mult).then_inc(last_h, 1)
            for half, c in enumerate(HALVES):
                dve.wait_ge(last_h_hi, half + 1)
                lo(h_lo[:, s % 2, c], h[:, s % 2, c], h_hi[:, s % 2, c], last_h_lo)
            parts = [scaled[:, d * TB:(d + 1) * TB] for d in range(K)]
            for d in range(K):
                dve.wait_ge(last_down, d + 1)
                c = coef[:, (NB - 1) * BPB:]
                c = bass.AP(c.tensor, c.offset, [c.ap[0], c.ap[1], [0, SEQ]])
                split = "p (b n) -> p b n"
                nc.vector.tensor_tensor(parts[d].rearrange(split, b=BPB), down_ps[:, d, :].rearrange(split, b=BPB), c,
                                        ALU.mult).then_inc(last_scaled, 1)
            for d in range(K):
                dve.wait_ge(last_scaled, d + 1)
                acc = out_acc[:, (NT - 1) * XB + d * TB:(NT - 1) * XB + (d + 1) * TB]
                nc.vector.tensor_tensor(acc, acc, parts[d], ALU.add).then_inc(last_acc, 1)


def kernel(x, fside_Bx8_0, condB_sharedgateprob, L0_cond_Wg, L0_cond_Wu, L0_cond_Wd, L0_cond_Sg, L0_cond_Su,
           L0_cond_Sd):
    import numpy as np
    import concourse.bacc as bacc
    from concourse.bass_utils import run_bass_kernel_spmd

    x, gating, shared, wg, wu, wd, sg, su, sd = (np.asarray(a) for a in (
        x, fside_Bx8_0, condB_sharedgateprob, L0_cond_Wg, L0_cond_Wu, L0_cond_Wd, L0_cond_Sg, L0_cond_Su,
        L0_cond_Sd))
    D, F = sg.shape
    K, NF, NE = D // P, F // P, wg.shape[0] + 1
    NT = x.size // D // TB
    xt = np.ascontiguousarray(x.reshape(NT, TB, K, P).transpose(0, 3, 2, 1))

    def columns(w, s):
        w = np.concatenate([w, s[None]]).reshape(NE, K, P, NF, P)
        return w.transpose(0, 3, 2, 1, 4)

    down = np.concatenate([wd, sd[None]]).reshape(NE, NF, P, K, P)
    w = np.concatenate([columns(wg, sg), columns(wu, su), down], axis=3)
    w = np.ascontiguousarray(w.reshape(NE, NF, P, 3 * K * P))

    nc = bacc.Bacc("TRN2", target_bir_lowering=False, num_devices=1)
    arrays = {"x_t": xt, "gating": np.ascontiguousarray(gating), "shared": np.ascontiguousarray(shared), "w": w}
    aps = [nc.dram_tensor(n, a.shape, F32, kind="ExternalInput").ap() for n, a in arrays.items()]
    out = nc.dram_tensor("out", xt.shape, F32, kind="ExternalOutput").ap()
    moe_program(nc, *aps, out)
    r = run_bass_kernel_spmd(nc, [arrays], core_ids=[0])
    got = r.results[0]["out"]
    return got.transpose(0, 3, 2, 1).reshape(x.shape)
```
